# Optimizing a Trainium2 kernel written in Bass

```python
import numpy as np
import jax
import jax.numpy as jnp

def _softmax(x, axis=-1):
    return jax.nn.softmax(x, axis=axis)

def _gelu(x):
    return jax.nn.gelu(x, approximate=True)

def _silu(x):
    return jax.nn.silu(x)

def _sigmoid(x):
    return jax.nn.sigmoid(x)

def _layernorm(x, axis=-1, eps=1e-05):
    m = jnp.mean(x, axis=axis, keepdims=True)
    v = jnp.var(x, axis=axis, keepdims=True)
    return (x - m) / jnp.sqrt(v + eps)

def _scatter_add(tgt, idx, src, axis=0):
    return tgt.at[idx].add(src)

def _segment_sum(src, seg, n):
    return jax.ops.segment_sum(src, seg, n)
kernel_name = 'mk_prb_d2_jaxref_r4_1a1d88'

def setup_inputs(seed: int=0):
    np.random.seed(seed)
    _w = jnp.asarray

    def _L0_attn_setup():
        import jax, jax.numpy as jnp
        import numpy as np
        EPS = 1e-06
        CHUNK = 64
        N_HEADS = 16
        GATE_NORM = 16.0

        def rmsnorm(x, eps=EPS):
            return x * jax.lax.rsqrt(jnp.mean(x * x, axis=-1, keepdims=True) + eps)

        def chunk_gate_retention(q, k, v, gt, chunk_size):
            b, h, t, d = q.shape
            c = chunk_size
            n = t // c
            scale = d ** (-0.5)
            q = q.reshape(b, h, n, c, d) * scale
            k = k.reshape(b, h, n, c, d)
            v = v.reshape(b, h, n, c, d)
            g = gt.reshape(b, h, n, c)
            bc = jnp.cumsum(g, axis=-1)
            B = bc[..., -1:]
            decay = jnp.exp(bc[..., :, None] - bc[..., None, :])
            mask = jnp.tril(jnp.ones((c, c), dtype=bool))
            A = jnp.einsum('bhnid,bhnjd->bhnij', q, k) * jnp.where(mask, decay, 0.0)
            o_intra = jnp.einsum('bhnij,bhnjd->bhnid', A, v)
            kd = k * jnp.exp(B - bc)[..., None]
            kv = jnp.einsum('bhncd,bhnce->bhnde', kd, v)
            qd = q * jnp.exp(bc)[..., None]

            def step(S, inp):
                qd_n, kv_n, B_n = inp
                o_cross = jnp.einsum('bhcd,bhde->bhce', qd_n, S)
                S_new = jnp.exp(B_n)[..., None] * S + kv_n
                return (S_new, o_cross)
            S0 = jnp.zeros((b, h, d, d), dtype=q.dtype)
            inps = (jnp.moveaxis(qd, 2, 0), jnp.moveaxis(kv, 2, 0), jnp.moveaxis(B, 2, 0))
            S_last, o_cross = jax.lax.scan(step, S0, inps)
            o_cross = jnp.moveaxis(o_cross, 0, 2)
            o = (o_intra + o_cross).reshape(b, h, t, d)
            return (o, S_last)
        key = jax.random.key(seed)
        ks = jax.random.split(key, 7)
        dim, nh = (256, N_HEADS)
        s = 0.03
        return {'x': jax.random.normal(ks[0], (2, 2048, dim), dtype=jnp.float32), 'Wq': jax.random.normal(ks[1], (dim, dim), dtype=jnp.float32) * s, 'Wk': jax.random.normal(ks[2], (dim, dim), dtype=jnp.float32) * s, 'Wv': jax.random.normal(ks[3], (dim, dim), dtype=jnp.float32) * s, 'Wg': jax.random.normal(ks[4], (dim, dim), dtype=jnp.float32) * s, 'Wgt': jax.random.normal(ks[5], (dim, nh), dtype=jnp.float32) * s, 'Wo': jax.random.normal(ks[6], (dim, dim), dtype=jnp.float32) * s}
    _L0_attn_in = _L0_attn_setup()

    def _L0_ffn_setup():
        import jax, jax.numpy as jnp
        import numpy as np
        TOP_K = 2
        key = jax.random.key(seed)
        k_x, k_g, k_w1, k_w2, k_w3 = jax.random.split(key, 5)
        B, S, D, H, E = (2, 128, 256, 128, 8)
        x = jax.random.normal(k_x, (B, S, D), dtype=jnp.float32)
        gate_w = jax.random.normal(k_g, (D, E), dtype=jnp.float32) * D ** (-0.5)
        w1 = jax.random.normal(k_w1, (E, D, H), dtype=jnp.float32) * 0.02
        w2 = jax.random.normal(k_w2, (E, H, D), dtype=jnp.float32) * 0.02
        w3 = jax.random.normal(k_w3, (E, D, H), dtype=jnp.float32) * 0.02
        return {'x': x, 'gate_w': gate_w, 'w1': w1, 'w2': w2, 'w3': w3}
    _L0_ffn_in = _L0_ffn_setup()

    def _L1_attn_setup():
        import jax, jax.numpy as jnp
        import numpy as np
        D_MODEL = 256
        D_STATE = 16
        D_CONV = 4
        EXPAND = 2
        D_INNER = D_MODEL * EXPAND
        BATCH = 2
        SEQ = 512

        def _silu(v):
            return v * jax.nn.sigmoid(v)
        key = jax.random.key(seed)
        ks = jax.random.split(key, 8)

        def rn(k, shape, scale):
            return jax.random.normal(k, shape, jnp.float32) * scale
        x = rn(ks[0], (BATCH, SEQ, D_MODEL), 1.0)
        W_in = rn(ks[1], (2 * D_INNER, D_MODEL), 0.02)
        conv_w = rn(ks[2], (D_INNER, 1, D_CONV), 0.2)
        conv_b = rn(ks[3], (D_INNER,), 0.02)
        W_x = rn(ks[4], (2 * D_STATE + 1, D_INNER), 0.02)
        W_dt = rn(ks[5], (D_INNER, 1), 0.5)
        b_dt = rn(ks[6], (D_INNER,), 0.02)
        A_log = jnp.log(jnp.broadcast_to(jnp.arange(1, D_STATE + 1, dtype=jnp.float32), (D_INNER, D_STATE)))
        D_param = jnp.ones((D_INNER,), jnp.float32)
        W_out = rn(ks[7], (D_MODEL, D_INNER), 0.02)
        return dict(x=x, W_in=W_in, conv_w=conv_w, conv_b=conv_b, W_x=W_x, W_dt=W_dt, b_dt=b_dt, A_log=A_log, D_param=D_param, W_out=W_out)
    _L1_attn_in = _L1_attn_setup()

    def _L1_ffn_setup():
        import jax, jax.numpy as jnp
        import numpy as np
        B, N, D = (4, 2048, 256)
        HEADS, DH = (8, 64)
        HID = HEADS * DH
        WIN = 128
        NQ, NKV = (256, 512)
        EPS, N_ITERS, FETCH_K = (1.0, 50, 9.0 / 8.0)
        SCALE = DH ** (-0.5)

        def rmsnorm(x, gamma):
            norm = jnp.maximum(jnp.linalg.norm(x, axis=-1, keepdims=True), 1e-12)
            return x / norm * x.shape[-1] ** 0.5 * gamma

        def coor_descent(s, k):
            logk = jnp.log(jnp.asarray(k, s.dtype))

            def body(_, ab):
                a, b = ab
                a = EPS * (logk - jax.nn.logsumexp((s + b) / EPS, axis=-1, keepdims=True))
                b = -jax.nn.relu(s + a)
                return (a, b)
            a, b = jax.lax.fori_loop(0, N_ITERS, body, (jnp.zeros_like(s[..., :1]), -s))
            return jnp.exp((s + a + b) / EPS)

        def route(x, routing_token, num_tokens):
            s = jnp.einsum('bnd,d->bn', x, routing_token)
            k = min(num_tokens * FETCH_K, x.shape[1])
            scores = coor_descent(s, k)
            sel_scores, sel_idx = jax.lax.top_k(scores, num_tokens)
            sel_scores = sel_scores + jax.lax.stop_gradient(1.0 - sel_scores)
            return (sel_scores, sel_idx)

        def light_local_attn(x, gamma, wq, wkv, wo):
            b, n, d = x.shape
            xn = rmsnorm(x, gamma)
            q = xn @ wq
            k, v = jnp.split(xn @ wkv, 2, axis=-1)

            def win(t):
                return t.reshape(b, n // WIN, WIN, HEADS, DH).transpose(0, 1, 3, 2, 4)
            q, k, v = (win(q) * SCALE, win(k), win(v))
            attn = jax.nn.softmax(jnp.einsum('bwhid,bwhjd->bwhij', q, k), axis=-1)
            out = jnp.einsum('bwhij,bwhjd->bwhid', attn, v)
            out = out.transpose(0, 1, 3, 2, 4).reshape(b, n, HID)
            return out @ wo

        def heavy_attn(xq, context, scores_kv, gamma, wq, wkv_t, wo):
            b, nq, d = xq.shape
            nkv = context.shape[1]
            xqn = rmsnorm(xq, gamma)
            ctx = rmsnorm(context, gamma)[:, None]
            q = (xqn @ wq).reshape(b, nq, HEADS, DH).transpose(0, 2, 1, 3) * SCALE
            kvw = wkv_t.reshape(1, HEADS, 2 * DH, d)
            kv = jnp.einsum('rhdi,brni->brhnd', kvw, ctx)
            k, v = jnp.split(kv, 2, axis=-1)
            v = v * scores_kv[:, None, None, :, None]
            k = k.reshape(b, HEADS, nkv, DH)
            v = v.reshape(b, HEADS, nkv, DH)
            attn = jax.nn.softmax(jnp.einsum('bhid,bhjd->bhij', q, k), axis=-1)
            out = jnp.einsum('bhij,bhjd->bhid', attn, v)
            out = out.transpose(0, 2, 1, 3).reshape(b, nq, HID)
            return out @ wo
        key = jax.random.key(seed)
        ks = jax.random.split(key, 10)
        lin = lambda k, shape, fan: jax.random.normal(k, shape, jnp.float32) * fan ** (-0.5)
        return dict(x=jax.random.normal(ks[0], (B, N, D), jnp.float32), gamma_light=jnp.ones((D,), jnp.float32), wq_light=lin(ks[1], (D, HID), D), wkv_light=lin(ks[2], (D, 2 * HID), D), wo_light=lin(ks[3], (HID, D), HID), q_routing_token=jax.random.normal(ks[4], (D,), jnp.float32), kv_routing_token=jax.random.normal(ks[5], (D,), jnp.float32), gamma_heavy=jnp.ones((D,), jnp.float32), wq_heavy=lin(ks[6], (D, HID), D), wkv_heavy=lin(ks[7], (2 * HID, D), D), wo_heavy=lin(ks[8], (HID, D), HID))
    _L1_ffn_in = _L1_ffn_setup()
    _d = {'L0_attn_x': _L0_attn_in['x'], 'L0_attn_Wq': _L0_attn_in['Wq'], 'L0_attn_Wk': _L0_attn_in['Wk'], 'L0_attn_Wv': _L0_attn_in['Wv'], 'L0_attn_Wg': _L0_attn_in['Wg'], 'L0_attn_Wgt': _L0_attn_in['Wgt'], 'L0_attn_Wo': _L0_attn_in['Wo'], 'L0_ffn_gate_w': _L0_ffn_in['gate_w'], 'L0_ffn_w1': _L0_ffn_in['w1'], 'L0_ffn_w2': _L0_ffn_in['w2'], 'L0_ffn_w3': _L0_ffn_in['w3'], 'L1_attn_W_in': _L1_attn_in['W_in'], 'L1_attn_conv_w': _L1_attn_in['conv_w'], 'L1_attn_conv_b': _L1_attn_in['conv_b'], 'L1_attn_W_x': _L1_attn_in['W_x'], 'L1_attn_W_dt': _L1_attn_in['W_dt'], 'L1_attn_b_dt': _L1_attn_in['b_dt'], 'L1_attn_A_log': _L1_attn_in['A_log'], 'L1_attn_D_param': _L1_attn_in['D_param'], 'L1_attn_W_out': _L1_attn_in['W_out'], 'L1_ffn_gamma_light': _L1_ffn_in['gamma_light'], 'L1_ffn_wq_light': _L1_ffn_in['wq_light'], 'L1_ffn_wkv_light': _L1_ffn_in['wkv_light'], 'L1_ffn_wo_light': _L1_ffn_in['wo_light'], 'L1_ffn_q_routing_token': _L1_ffn_in['q_routing_token'], 'L1_ffn_kv_routing_token': _L1_ffn_in['kv_routing_token'], 'L1_ffn_gamma_heavy': _L1_ffn_in['gamma_heavy'], 'L1_ffn_wq_heavy': _L1_ffn_in['wq_heavy'], 'L1_ffn_wkv_heavy': _L1_ffn_in['wkv_heavy'], 'L1_ffn_wo_heavy': _L1_ffn_in['wo_heavy']}
    _x0 = _d['L0_attn_x']
    _d['L0_attn_x'] = jax.random.normal(jax.random.fold_in(jax.random.key(seed), 1), (8, 512, 256), dtype=_x0.dtype)
    del _x0
    return _d

def reference(L0_attn_x, L0_attn_Wq, L0_attn_Wk, L0_attn_Wv, L0_attn_Wg, L0_attn_Wgt, L0_attn_Wo, L0_ffn_gate_w, L0_ffn_w1, L0_ffn_w2, L0_ffn_w3, L1_attn_W_in, L1_attn_conv_w, L1_attn_conv_b, L1_attn_W_x, L1_attn_W_dt, L1_attn_b_dt, L1_attn_A_log, L1_attn_D_param, L1_attn_W_out, L1_ffn_gamma_light, L1_ffn_wq_light, L1_ffn_wkv_light, L1_ffn_wo_light, L1_ffn_q_routing_token, L1_ffn_kv_routing_token, L1_ffn_gamma_heavy, L1_ffn_wq_heavy, L1_ffn_wkv_heavy, L1_ffn_wo_heavy):

    def _L0_attn_ref(x, Wq, Wk, Wv, Wg, Wgt, Wo):
        import jax, jax.numpy as jnp
        import numpy as np
        EPS = 1e-06
        CHUNK = 64
        N_HEADS = 16
        GATE_NORM = 16.0

        def rmsnorm(x, eps=EPS):
            return x * jax.lax.rsqrt(jnp.mean(x * x, axis=-1, keepdims=True) + eps)

        def chunk_gate_retention(q, k, v, gt, chunk_size):
            b, h, t, d = q.shape
            c = chunk_size
            n = t // c
            scale = d ** (-0.5)
            q = q.reshape(b, h, n, c, d) * scale
            k = k.reshape(b, h, n, c, d)
            v = v.reshape(b, h, n, c, d)
            g = gt.reshape(b, h, n, c)
            bc = jnp.cumsum(g, axis=-1)
            B = bc[..., -1:]
            decay = jnp.exp(bc[..., :, None] - bc[..., None, :])
            mask = jnp.tril(jnp.ones((c, c), dtype=bool))
            A = jnp.einsum('bhnid,bhnjd->bhnij', q, k) * jnp.where(mask, decay, 0.0)
            o_intra = jnp.einsum('bhnij,bhnjd->bhnid', A, v)
            kd = k * jnp.exp(B - bc)[..., None]
            kv = jnp.einsum('bhncd,bhnce->bhnde', kd, v)
            qd = q * jnp.exp(bc)[..., None]

            def step(S, inp):
                qd_n, kv_n, B_n = inp
                o_cross = jnp.einsum('bhcd,bhde->bhce', qd_n, S)
                S_new = jnp.exp(B_n)[..., None] * S + kv_n
                return (S_new, o_cross)
            S0 = jnp.zeros((b, h, d, d), dtype=q.dtype)
            inps = (jnp.moveaxis(qd, 2, 0), jnp.moveaxis(kv, 2, 0), jnp.moveaxis(B, 2, 0))
            S_last, o_cross = jax.lax.scan(step, S0, inps)
            o_cross = jnp.moveaxis(o_cross, 0, 2)
            o = (o_intra + o_cross).reshape(b, h, t, d)
            return (o, S_last)
        b, t, dim = x.shape
        h = N_HEADS
        d = dim // h
        q = rmsnorm(x @ Wq)
        k = rmsnorm(x @ Wk)
        v = rmsnorm(x @ Wv)
        g = x @ Wg
        gt = jax.nn.log_sigmoid(x @ Wgt) / GATE_NORM
        qr = q.reshape(b, t, h, d).transpose(0, 2, 1, 3)
        kr = k.reshape(b, t, h, d).transpose(0, 2, 1, 3)
        vr = v.reshape(b, t, h, d).transpose(0, 2, 1, 3)
        gtr = gt.transpose(0, 2, 1)
        o, _ = chunk_gate_retention(qr, kr, vr, gtr, CHUNK)
        o = rmsnorm(o)
        o = o.transpose(0, 2, 1, 3).reshape(b, t, dim)
        o = jax.nn.silu(g) * o
        return o @ Wo

    def _L0_ffn_ref(x, gate_w, w1, w2, w3):
        import jax, jax.numpy as jnp
        import numpy as np
        TOP_K = 2
        B, S, D = x.shape
        E = gate_w.shape[1]
        xf = x.reshape(B * S, D)
        T = B * S
        logits = xf @ gate_w
        scores = jax.nn.softmax(logits, axis=-1)
        top_scores, top_idx = jax.lax.top_k(scores, TOP_K)
        scale = jnp.zeros((T, E), dtype=x.dtype).at[jnp.arange(T)[:, None], top_idx].set(top_scores)
        xs = scale.T[:, :, None] * xf[None, :, :]
        h = jax.nn.silu(jnp.einsum('etd,edh->eth', xs, w1)) * jnp.einsum('etd,edh->eth', xs, w3)
        y = jnp.einsum('eth,ehd->etd', h, w2)
        out = y.sum(axis=0)
        return out.reshape(B, S, D)

    def _L1_attn_ref(x, W_in, conv_w, conv_b, W_x, W_dt, b_dt, A_log, D_param, W_out):
        import jax, jax.numpy as jnp
        import numpy as np
        D_MODEL = 256
        D_STATE = 16
        D_CONV = 4
        EXPAND = 2
        D_INNER = D_MODEL * EXPAND
        BATCH = 2
        SEQ = 512

        def _silu(v):
            return v * jax.nn.sigmoid(v)
        B, T, _ = x.shape
        xz = jnp.einsum('btm,im->bti', x, W_in)
        x_d, z = jnp.split(xz, 2, axis=-1)
        xc = jnp.moveaxis(x_d, 1, 2)
        xc = jnp.pad(xc, ((0, 0), (0, 0), (D_CONV - 1, 0)))
        xc = jax.lax.conv_general_dilated(xc, conv_w, window_strides=(1,), padding='VALID', feature_group_count=D_INNER, dimension_numbers=('NCH', 'OIH', 'NCH'))
        x_d = _silu(jnp.moveaxis(xc + conv_b[None, :, None], 1, 2))
        A = -jnp.exp(A_log)
        ssm_in = jnp.einsum('btd,kd->btk', x_d, W_x)
        dt_raw = ssm_in[..., :1]
        B_mat = ssm_in[..., 1:1 + D_STATE]
        C_mat = ssm_in[..., 1 + D_STATE:]
        delta = jax.nn.softplus(dt_raw * W_dt[:, 0] + b_dt)

        def step(h, inp):
            d_t, b_t, c_t, u_t = inp
            dA = jnp.exp(d_t[..., None] * A)
            h = dA * h + d_t[..., None] * b_t[:, None, :] * u_t[..., None]
            y = jnp.einsum('bds,bs->bd', h, c_t)
            return (h, y)
        h0 = jnp.zeros((B, D_INNER, D_STATE), x.dtype)
        xs = (jnp.moveaxis(delta, 1, 0), jnp.moveaxis(B_mat, 1, 0), jnp.moveaxis(C_mat, 1, 0), jnp.moveaxis(x_d, 1, 0))
        _, ys = jax.lax.scan(step, h0, xs)
        y = jnp.moveaxis(ys, 0, 1) + D_param * x_d
        y = y * _silu(z)
        return jnp.einsum('btd,md->btm', y, W_out)

    def _L1_ffn_ref(x, gamma_light, wq_light, wkv_light, wo_light, q_routing_token, kv_routing_token, gamma_heavy, wq_heavy, wkv_heavy, wo_heavy):
        import jax, jax.numpy as jnp
        import numpy as np
        B, N, D = (4, 2048, 256)
        HEADS, DH = (8, 64)
        HID = HEADS * DH
        WIN = 128
        NQ, NKV = (256, 512)
        EPS, N_ITERS, FETCH_K = (1.0, 50, 9.0 / 8.0)
        SCALE = DH ** (-0.5)

        def rmsnorm(x, gamma):
            norm = jnp.maximum(jnp.linalg.norm(x, axis=-1, keepdims=True), 1e-12)
            return x / norm * x.shape[-1] ** 0.5 * gamma

        def coor_descent(s, k):
            logk = jnp.log(jnp.asarray(k, s.dtype))

            def body(_, ab):
                a, b = ab
                a = EPS * (logk - jax.nn.logsumexp((s + b) / EPS, axis=-1, keepdims=True))
                b = -jax.nn.relu(s + a)
                return (a, b)
            a, b = jax.lax.fori_loop(0, N_ITERS, body, (jnp.zeros_like(s[..., :1]), -s))
            return jnp.exp((s + a + b) / EPS)

        def route(x, routing_token, num_tokens):
            s = jnp.einsum('bnd,d->bn', x, routing_token)
            k = min(num_tokens * FETCH_K, x.shape[1])
            scores = coor_descent(s, k)
            sel_scores, sel_idx = jax.lax.top_k(scores, num_tokens)
            sel_scores = sel_scores + jax.lax.stop_gradient(1.0 - sel_scores)
            return (sel_scores, sel_idx)

        def light_local_attn(x, gamma, wq, wkv, wo):
            b, n, d = x.shape
            xn = rmsnorm(x, gamma)
            q = xn @ wq
            k, v = jnp.split(xn @ wkv, 2, axis=-1)

            def win(t):
                return t.reshape(b, n // WIN, WIN, HEADS, DH).transpose(0, 1, 3, 2, 4)
            q, k, v = (win(q) * SCALE, win(k), win(v))
            attn = jax.nn.softmax(jnp.einsum('bwhid,bwhjd->bwhij', q, k), axis=-1)
            out = jnp.einsum('bwhij,bwhjd->bwhid', attn, v)
            out = out.transpose(0, 1, 3, 2, 4).reshape(b, n, HID)
            return out @ wo

        def heavy_attn(xq, context, scores_kv, gamma, wq, wkv_t, wo):
            b, nq, d = xq.shape
            nkv = context.shape[1]
            xqn = rmsnorm(xq, gamma)
            ctx = rmsnorm(context, gamma)[:, None]
            q = (xqn @ wq).reshape(b, nq, HEADS, DH).transpose(0, 2, 1, 3) * SCALE
            kvw = wkv_t.reshape(1, HEADS, 2 * DH, d)
            kv = jnp.einsum('rhdi,brni->brhnd', kvw, ctx)
            k, v = jnp.split(kv, 2, axis=-1)
            v = v * scores_kv[:, None, None, :, None]
            k = k.reshape(b, HEADS, nkv, DH)
            v = v.reshape(b, HEADS, nkv, DH)
            attn = jax.nn.softmax(jnp.einsum('bhid,bhjd->bhij', q, k), axis=-1)
            out = jnp.einsum('bhij,bhjd->bhid', attn, v)
            out = out.transpose(0, 2, 1, 3).reshape(b, nq, HID)
            return out @ wo
        b = x.shape[0]
        light_out = light_local_attn(x, gamma_light, wq_light, wkv_light, wo_light)
        scores_q, idx_q = route(x, q_routing_token, NQ)
        scores_kv, idx_kv = route(x, kv_routing_token, NKV)
        routed_q = jnp.take_along_axis(x, idx_q[..., None], axis=1)
        routed_kv = jnp.take_along_axis(x, idx_kv[..., None], axis=1)
        routed_out = heavy_attn(routed_q, routed_kv, scores_kv, gamma_heavy, wq_heavy, wkv_heavy, wo_heavy)
        routed_out = routed_out * scores_q[..., None]
        heavy_out = jnp.zeros_like(x).at[jnp.arange(b)[:, None], idx_q].set(routed_out)
        return light_out + heavy_out
    x = L0_attn_x
    xn = _layernorm(x, axis=-1)
    x = x + _L0_attn_ref(xn, L0_attn_Wq, L0_attn_Wk, L0_attn_Wv, L0_attn_Wg, L0_attn_Wgt, L0_attn_Wo) + _L0_ffn_ref(xn, L0_ffn_gate_w, L0_ffn_w1, L0_ffn_w2, L0_ffn_w3)
    xn = _layernorm(x, axis=-1)
    x = x + _L1_attn_ref(xn, L1_attn_W_in, L1_attn_conv_w, L1_attn_conv_b, L1_attn_W_x, L1_attn_W_dt, L1_attn_b_dt, L1_attn_A_log, L1_attn_D_param, L1_attn_W_out) + _L1_ffn_ref(xn, L1_ffn_gamma_light, L1_ffn_wq_light, L1_ffn_wkv_light, L1_ffn_wo_light, L1_ffn_q_routing_token, L1_ffn_kv_routing_token, L1_ffn_gamma_heavy, L1_ffn_wq_heavy, L1_ffn_wkv_heavy, L1_ffn_wo_heavy)
    return x

_drawn_inputs = setup_inputs


def setup_inputs(seed=0):
    import zlib

    import numpy as np

    out = dict(_drawn_inputs(seed))
    spreads = {'L1_attn_D_param': (1.0, 0.2),
     'L1_ffn_gamma_light': (1.0, 0.2),
     'L1_ffn_gamma_heavy': (1.0, 0.2)}
    factors = {}
    for name, (base, spread) in spreads.items():
        noise = np.random.default_rng([zlib.crc32(name.encode()), seed]).standard_normal(out[name].shape)
        drawn = base * np.exp(spread * noise) if base else spread * noise
        out[name] = jnp.asarray(drawn.astype(out[name].dtype))
    for name, factor in factors.items():
        out[name] = (out[name] * factor).astype(out[name].dtype)
    return out
```

```python
from contextlib import ExitStack

import numpy as np

import concourse.bass as bass
from concourse import mybir
from concourse.alu_op_type import AluOpType as ALU

F32 = mybir.dt.float32
ACT = mybir.ActivationFunctionType
X_AXIS = mybir.AxisListType.X

P = 128
B, T, D = 8, 512, 256
NT = T // P
ND = D // P

H, HD, CH = 16, 16, 64
HG = 4
E, HID = 8, 128
EG = 2
DI, DS, CONV = 512, 16, 4
NB = DI // P
AH, DH = 8, 64
HIDA = AH * DH
NA = HIDA // P
NQ = 256
K_FETCH = NQ * 9 / 8
ROUTE_ITERS = 50
LN_EPS, RMS_EPS = 1e-5, 1e-6
LN_EXP_TABLE = 6


class Own:

    def __init__(self, eng, sem):
        self.eng, self.sem, self.n = eng, sem, 0

    def __call__(self, ins):
        ins.then_inc(self.sem, 1)
        self.n += 1
        return self.n

    def need(self, n):
        self.eng.wait_ge(self.sem, n)

    def now(self, ins):
        self.need(self(ins))


def bc(ap, n):
    ap = ap.unsqueeze(len(ap.shape))
    return ap.broadcast_to([*ap.shape[:-1], n])


def mid(ap, n):
    p, a = ap.shape
    return ap.unsqueeze(1).broadcast_to([p, n, a])


def clear(nc, sems):
    nums = [s.num for s in sems.values()]
    nc.gpsimd.sem_clear(range(min(nums), max(nums) + 1))
    nc.all_engine_barrier()


def layer0(nc, x, w, scr, PB, const, load_ln_exp):
    ctx = ExitStack()
    with ctx:
        def sb(name, shape):
            return ctx.enter_context(nc.sbuf_tensor(name, [P, *shape], F32))

        Wqk, Wvg, Wsm = sb("Wqk", [ND, 2 * D]), sb("Wvg", [ND, 2 * D]), sb("Wsm", [ND, H + E])
        Wo, W1, W3 = sb("Wo", [ND, D]), sb("W1", [ND, E, HID]), sb("W3", [ND, E, HID])
        W2 = sb("W2", [E, D])
        tok = sb("tok", [D])
        suffix, prefix = sb("suffix", [P]), sb("prefix", [P])
        chunk0, chunk1 = sb("chunk0", [P]), sb("chunk1", [P])
        tri, bdmask, before = sb("tri", [CH]), sb("bdmask", [CH]), sb("before", [E, E])
        half = sb("half", [P])
        X, XN, XT = sb("X", [NT, D]), sb("XN", [NT, D]), sb("XT", [ND, T])
        st, mv = sb("st", [NT, 6]), sb("mv", [NT, 2])
        ve, rstd = sb("ve", [NT]), sb("rstd", [NT])
        Qp, Kp = sb("Qp", [NT, H, 32]), sb("Kp", [NT, H, 32])
        VG, SM = sb("VG", [NT, 2 * D]), sb("SM", [NT, H + E])
        QT, KT = sb("QT", [NT, HG, P]), sb("KT", [NT, HG, P])
        ssq, rfac, fkv, fq = sb("ssq", [NT, 3]), sb("rfac", [NT, 3]), sb("fkv", [NT]), sb("fq", [NT])
        la, le, ll, gt = (sb(n, [NT, H]) for n in ("la", "le", "ll", "gt"))
        gm, ge, gs, gc = sb("gm", [NT]), sb("ge", [NT, E]), sb("gs", [NT]), sb("gc", [NT, E])
        cmp1, cmp2, SC = sb("cmp1", [NT * E, E]), sb("cmp2", [NT * E, E]), sb("SC", [NT, E])
        gU, dec, AT = sb("gU", [2, H, CH]), sb("dec", [NT, H, CH]), sb("AT", [2, 4, HG, CH])
        ER = sb("ER", [4, NT, H])
        v1, v2 = sb("v1", [NT, D]), sb("v2", [NT, D])
        S, kvm, sdec = sb("S", [2 * NT, D]), sb("kvm", [2, D]), sb("sdec", [D])
        O, SQ, hs, hr = sb("O", [NT, D]), sb("SQ", [NT, D]), sb("hs", [NT, H]), sb("hr", [NT, H])
        SG, OGT = sb("SG", [NT, D]), sb("OGT", [ND, T])
        HS, HH, HT = sb("HS", [2, 4, HID]), sb("HH", [2, 4, HID]), sb("HT", [2, 4, P])
        S2 = sb("S2", [NT])
        junk, prod = sb("junk", [2, 3, D]), sb("prod", [NT, D])

        names = """w_in own_v own_a own_g x_in xn_tm xT_ps xT_sb qk_ps vg_ps sm_ps qk_tm vg_tm sm_tm
            qT_ps kT_ps qT_sb kT_sb var ssq_a ssq_v pow_g gt_v glog_a gmax_v gexp_a gU_g sums_ps er_a
            arg_ps dec_raw dec_g v1_v v2_v sc_ps at_v kv_ps S_v o_ps o_v sq_a sg_a og_v ogT_ps ogT_sb
            wo_ps sc_v kvm_v hs_v xn2_v h_ps hs_a h_v hT_ps hT_sb y_ps y_v x1_v s_v stored"""
        s = {n: ctx.enter_context(nc.semaphore("a_" + n)) for n in names.split()}

        with nc.Block() as block:
            @block.sync
            def _(sp):
                loads = [
                    (Wqk[:, :, 0:D], w["L0_attn_Wq"].rearrange("(k p) n -> p k n", p=P)),
                    (Wqk[:, :, D:2 * D], w["L0_attn_Wk"].rearrange("(k p) n -> p k n", p=P)),
                    (Wvg[:, :, 0:D], w["L0_attn_Wv"].rearrange("(k p) n -> p k n", p=P)),
                    (Wvg[:, :, D:2 * D], w["L0_attn_Wg"].rearrange("(k p) n -> p k n", p=P)),
                    (Wsm[:, :, 0:H], w["L0_attn_Wgt"].rearrange("(k p) n -> p k n", p=P)),
                    (Wsm[:, :, H:H + E], w["L0_ffn_gate_w"].rearrange("(k p) n -> p k n", p=P)),
                    (Wo[:], w["L0_attn_Wo"].rearrange("(k p) n -> p k n", p=P)),
                    (W2[:], w["L0_ffn_w2"].rearrange("e p n -> p e n")),
                    (tok[:], w["L1_ffn_q_routing_token"].rearrange("(o d) -> o d", o=1).broadcast_to([P, D])),
                ]
                for k in range(ND):
                    for dst, name in ((W1, "L0_ffn_w1"), (W3, "L0_ffn_w3")):
                        loads.append((dst[:, k], w[name][:, k * P:(k + 1) * P, :].rearrange("e p n -> p e n")))
                for dst, src in loads:
                    sp.dma_start(dst, src).then_inc(s["w_in"], 16)
                sp.wait_ge(s["w_in"], 16 * len(loads))

            @block.gpsimd
            def _(pool):
                own = Own(pool, s["own_g"])
                for t, v in ((Qp, 0.0), (Kp, 0.0), (suffix, 1.0), (prefix, 1.0), (chunk0, 1.0),
                             (chunk1, 0.0), (tri, 1.0), (bdmask, 1.0), (before, 1.0), (half, -0.5)):
                    own(pool.memset(t[:], v))
                own(pool.memset(S[:, 0], 0.0))
                own.need(own.n)
                own.now(pool.memset(chunk0[CH:P], 0.0))
                own.now(pool.memset(chunk1[CH:P], 1.0))
                own.now(pool.affine_select(out=suffix[:], in_=suffix[:], compare_op=ALU.is_gt, fill=0.0, base=0,
                                       pattern=[[-1, P]], channel_multiplier=1))
                own.now(pool.affine_select(out=prefix[:], in_=prefix[:], compare_op=ALU.is_ge, fill=0.0, base=0,
                                       pattern=[[1, P]], channel_multiplier=-1))
                for c in range(2):
                    own.now(pool.affine_select(out=tri[c * CH:(c + 1) * CH], in_=tri[c * CH:(c + 1) * CH],
                                           compare_op=ALU.is_ge, fill=0.0, base=0,
                                           pattern=[[1, CH]], channel_multiplier=-1))
                for r in range(4):
                    q = bdmask[32 * r:32 * r + 32]
                    own.now(pool.memset(q, 0.0))
                    own.now(pool.memset(q[:, HD * r:HD * (r + 1)], 1.0))
                own.now(pool.affine_select(out=before[:], in_=before[:], compare_op=ALU.is_gt, fill=0.0, base=0,
                                       pattern=[[1, E], [-1, E]], channel_multiplier=0))
                own.now(pool.memset(suffix[CH:P, 0:CH], 0.0))
                own.now(pool.memset(prefix[0:CH, CH:P], 0.0))
        clear(nc, s)

        ident = const["ident"]
        with nc.Fori(0, B) as b:
          with nc.Block() as block:
            @block.sync
            def _(sp):
                def rows_of(name, t):
                    return scr[name][bass.ds(b, 1), t * P:(t + 1) * P, :].rearrange("o p d -> p (o d)")

                sp.dma_start(X[:], x[bass.ds(b, 1), :, :].rearrange("o (t p) d -> p (o t) d", p=P)) \
                  .then_inc(s["x_in"], 16)
                for t in range(NT):
                    sp.wait_ge(s["x1_v"], t + 1)
                    sp.dma_start(rows_of("x1", t), X[:, t]).then_inc(s["stored"], 16)
                    sp.wait_ge(s["xn2_v"], t + 1)
                    sp.dma_start(rows_of("xn2", t), XN[:, t]).then_inc(s["stored"], 16)
                sp.wait_ge(s["s_v"], NT)
                sp.dma_start(scr["s"][bass.ds(b, 1), :, :].rearrange("o p t -> p (o t)"), S2[:]) \
                  .then_inc(s["stored"], 16)
                sp.wait_ge(s["stored"], 16 * (2 * NT + 1))

            @block.gpsimd
            def _(pool):
                def power(out, base, after, value):
                    pool.wait_ge(s[after], value)
                    pool.tensor_tensor(out, base, half[:, 0:base.shape[1]], ALU.pow).then_inc(s["pow_g"], 1)

                def gates(t):
                    if t >= 2:
                        pool.wait_ge(s["arg_ps"], 2 * (t - 1))
                    pool.tensor_tensor(gU[:, t % 2], bc(gt[:, t], CH), mid(tri[:], H), ALU.mult) \
                        .then_inc(s["gU_g"], 1)

                def mask_decay(t):
                    pool.wait_ge(s["dec_raw"], 2 * (t + 1))
                    pool.tensor_tensor(dec[:, t], dec[:, t], mid(tri[:], H), ALU.mult).then_inc(s["dec_g"], 1)

                power(rstd[:], ve[:], "var", 1)
                pool.wait_ge(s["gt_v"], 1)
                gates(0)
                gates(1)
                gates(2)
                mask_decay(0)
                gates(3)
                power(rfac[:].rearrange("p t c -> p (t c)"), ssq[:].rearrange("p t c -> p (t c)"), "ssq_v", 1)
                for t in range(1, NT):
                    mask_decay(t)
                for t in range(NT):
                    power(hr[:, t], hs[:, t], "hs_v", t + 1)
                    power(rstd[:, t:t + 1], ve[:, t:t + 1], "var", t + 2)

            @block.tensor
            def _(pe):
                def mm(out, lhsT, rhs, start=True, stop=True):
                    return pe.matmul(out, lhsT, rhs, start=start, stop=stop)

                for t in range(NT):
                    pe.wait_ge(s["xn_tm"], t + 1)
                    for k in range(ND):
                        q = pe.transpose(PB[k][:, t * P:(t + 1) * P], XN[:, t, k * P:(k + 1) * P], ident[:])
                q.then_inc(s["xT_ps"], 1)
                pe.wait_ge(s["xT_sb"], 2)

                for t in range(NT):
                    for k in range(ND):
                        q = mm(PB[6][:, t * (H + E):(t + 1) * (H + E)], XT[:, k, t * P:(t + 1) * P], Wsm[:, k],
                               k == 0, k == ND - 1)
                q.then_inc(s["sm_ps"], 1)

                def turn(t):
                    pe.wait_ge(s["qk_tm"], t + 1)
                    for bank, src, done, out in ((0, Qp, "qT_sb", "qT_ps"), (1, Kp, "kT_sb", "kT_ps")):
                        if t >= 1:
                            pe.wait_ge(s[done], t)
                        for g in range(HG):
                            q = pe.transpose(PB[bank][:, g * P:(g + 1) * P],
                                             src[:, t, 4 * g:4 * g + 4].rearrange("p h c -> p (h c)"), ident[:])
                        q.then_inc(s[out], 1)

                def decays(t):
                    pe.wait_ge(s["gU_g"], t + 1)
                    for g in range(2):
                        if t:
                            pe.wait_ge(s["dec_raw"], 2 * t - 1 + g)
                        else:
                            pe.wait_ge(s["er_a" if g else "sm_tm"], 1)
                        mm(PB[6 + g][:], suffix[:], gU[:, t % 2, 8 * g:8 * g + 8].rearrange("p h i -> p (h i)")) \
                            .then_inc(s["arg_ps"], 1)

                for t in range(NT):
                    if t >= 2:
                        pe.wait_ge(s["qk_tm"], t - 1)
                        pe.wait_ge(s["vg_tm"], t - 1)
                    for k in range(ND):
                        q = mm(PB[2 + t % 2][:], XT[:, k, t * P:(t + 1) * P], Wqk[:, k], k == 0, k == ND - 1)
                    q.then_inc(s["qk_ps"], 1)
                    for k in range(ND):
                        q = mm(PB[4 + t % 2][:], XT[:, k, t * P:(t + 1) * P], Wvg[:, k], k == 0, k == ND - 1)
                    q.then_inc(s["vg_ps"], 1)
                    if t == 0:
                        pe.wait_ge(s["gt_v"], 1)
                        for i, m in enumerate((suffix, prefix, chunk0, chunk1)):
                            q = mm(PB[7][:, i * NT * H:(i + 1) * NT * H], m[:], gt[:].rearrange("p t h -> p (t h)"))
                        q.then_inc(s["sums_ps"], 1)
                    else:
                        turn(t - 1)
                        decays(t - 1)
                turn(NT - 1)
                decays(NT - 1)

                def scores(t):
                    if t == 0:
                        pe.wait_ge(s["vg_tm"], NT)
                        pe.wait_ge(s["dec_raw"], 2 * NT)
                        pe.wait_ge(s["qT_sb"], NT)
                        pe.wait_ge(s["kT_sb"], NT)
                    else:
                        pe.wait_ge(s["at_v"], t)
                    for c in range(2):
                        cols = slice(c * CH, (c + 1) * CH)
                        for g in range(HG):
                            for r in range(4):
                                q = mm(PB[4 + r][cols, g * CH:(g + 1) * CH], KT[32 * r:32 * r + HD, t, g, cols],
                                       QT[32 * r:32 * r + HD, t, g, cols])
                    q.then_inc(s["sc_ps"], 1)

                def outer(t):
                    pe.wait_ge(s["v2_v"], t + 1)
                    if t:
                        pe.wait_ge(s["h_v"], 2 * t)
                        pe.wait_ge(s["y_v"], 2 * t)
                    else:
                        pe.wait_ge(s["qk_tm"], NT)
                        pe.wait_ge(s["kT_sb"], NT)
                    for c in range(2 if t < NT - 1 else 1):
                        rows = slice(c * CH, (c + 1) * CH)
                        for g in range(HG):
                            q = mm(PB[(3, 1)[c]][:, g * CH:(g + 1) * CH],
                                   Kp[rows, t, 4 * g:4 * g + 4].rearrange("p h c -> p (h c)"),
                                   v2[rows, t, g * CH:(g + 1) * CH])
                    q.then_inc(s["kv_ps"], 1)

                def up(n):
                    t, g = divmod(n, EG)
                    if n:
                        pe.wait_ge(s["h_v"], n)
                    if g == 0:
                        pe.wait_ge(s["kvm_v"], t + 1)
                    for bank, W in ((2, W1), (3, W3)):
                        for k in range(ND):
                            q = mm(PB[bank][:], XT[:, k, t * P:(t + 1) * P],
                                   W[:, k, 4 * g:4 * g + 4].rearrange("p e h -> p (e h)"), k == 0, k == ND - 1)
                    q.then_inc(s["h_ps"], 1)

                def turn_hidden(n):
                    pe.wait_ge(s["h_v"], n + 1)
                    if n:
                        pe.wait_ge(s["y_v"], n)
                    for e in range(4):
                        q = pe.transpose(PB[1][:, e * P:(e + 1) * P], HH[:, n % 2, e], ident[:])
                    q.then_inc(s["hT_ps"], 1)

                def down(n):
                    g = n % EG
                    pe.wait_ge(s["hT_sb"], n + 1)
                    for e in range(4):
                        q = mm(PB[1][:, 0:D], HT[:, n % 2, e], W2[:, 4 * g + e], e == 0, e == 3)
                    q.then_inc(s["y_ps"], 1)

                scores(0)
                outer(0)
                for t in range(NT):
                    up(EG * t)
                    pe.wait_ge(s["at_v"], t + 1)
                    if t:
                        pe.wait_ge(s["x1_v"], t)
                    for c in range(2):
                        rows = slice(c * CH, (c + 1) * CH)
                        for h in range(H):
                            q = mm(PB[0][rows, h * HD:(h + 1) * HD], AT[rows, t % 2, h % 4, h // 4],
                                   v1[rows, t, h * HD:(h + 1) * HD])
                    for c in range(2):
                        rows, n = slice(c * CH, (c + 1) * CH), 2 * t + c
                        if n:
                            pe.wait_ge(s["S_v"], n)
                        for g in range(HG):
                            q = mm(PB[0][rows, D + g * CH:D + (g + 1) * CH], QT[:, t, g, rows],
                                   S[:, n, g * CH:(g + 1) * CH])
                    q.then_inc(s["o_ps"], 1)
                    turn_hidden(EG * t)
                    up(EG * t + 1)
                    down(EG * t)
                    if t < NT - 1:
                        scores(t + 1)
                    turn_hidden(EG * t + 1)
                    pe.wait_ge(s["og_v"], t + 1)
                    for k in range(ND):
                        q = pe.transpose(PB[0][:, k * P:(k + 1) * P], O[:, t, k * P:(k + 1) * P], ident[:])
                    q.then_inc(s["ogT_ps"], 1)
                    down(EG * t + 1)
                    pe.wait_ge(s["ogT_sb"], t + 1)
                    for k in range(ND):
                        q = mm(PB[0][:, D:2 * D], OGT[:, k, t * P:(t + 1) * P], Wo[:, k], k == 0, k == ND - 1)
                    q.then_inc(s["wo_ps"], 1)
                    if t < NT - 1:
                        outer(t + 1)

            @block.scalar
            def _(act):
                own = Own(act, s["own_a"])
                load_ln_exp(act)
                act.wait_ge(s["xT_ps"], 1)
                act.activation(XT[:, 0], PB[0][:], ACT.Copy).then_inc(s["xT_sb"], 1)
                act.wait_ge(s["sm_tm"], 1)
                own.now(act.activation(la[:], SM[:, :, 0:H], ACT.Abs))
                own.now(act.activation(le[:], la[:], ACT.Exp, scale=-1.0))
                act.activation(ll[:], le[:], ACT.Ln, bias=1.0).then_inc(s["glog_a"], 1)

                def turn_and_decay(t):
                    act.wait_ge(s["qT_ps"], t + 1)
                    act.activation(QT[:, t].rearrange("p g i -> p (g i)"), PB[0][:], ACT.Copy) \
                        .then_inc(s["qT_sb"], 1)
                    for g in range(2):
                        act.wait_ge(s["arg_ps"], 2 * t + g + 1)
                        act.activation(dec[:, t, 8 * g:8 * g + 8].rearrange("p h i -> p (h i)"),
                                       PB[6 + g][:], ACT.Exp).then_inc(s["dec_raw"], 1)

                for t in range(NT):
                    act.wait_ge(s["qk_ps"], t + 1)
                    if t >= 2:
                        act.wait_ge(s["ssq_a"], t - 1)
                    for i, dst in enumerate((Qp, Kp)):
                        src = PB[2 + t % 2][:, i * D:(i + 1) * D]
                        act.activation(dst[:, t, :, 0:HD], src.rearrange("p (h e) -> p h e", h=H), ACT.Copy)
                        q = act.activation(junk[:, t % 2, i], src, ACT.Square, accum_out=ssq[:, t, i:i + 1])
                    q.then_inc(s["qk_tm"], 1)
                    act.wait_ge(s["vg_tm"], t + 1)
                    act.activation(junk[:, t % 2, 2], VG[:, t, 0:D], ACT.Square, accum_out=ssq[:, t, 2:3]) \
                        .then_inc(s["ssq_a"], 1)
                    if t == 0:
                        act.wait_ge(s["gmax_v"], 1)
                        act.activation(ge[:], gc[:], ACT.Exp).then_inc(s["gexp_a"], 1)
                        act.wait_ge(s["sums_ps"], 1)
                        act.activation(ER[:].rearrange("p i t h -> p (i t h)"), PB[7][:, 0:4 * NT * H], ACT.Exp) \
                            .then_inc(s["er_a"], 1)
                    else:
                        turn_and_decay(t - 1)
                turn_and_decay(NT - 1)
                act.activation(SG[:], VG[:, :, D:2 * D], ACT.Silu).then_inc(s["sg_a"], 1)

                def silu(n):
                    t, g = divmod(n, EG)
                    act.wait_ge(s["h_ps"], n + 1)
                    if n >= 2:
                        act.wait_ge(s["h_v"], n - 1)
                    for e in range(4):
                        q = act.activation(HS[:, n % 2, e], PB[2][:, e * HID:(e + 1) * HID],
                                           ACT.Silu, scale=SC[:, t, 4 * g + e:4 * g + e + 1])
                    q.then_inc(s["hs_a"], 1)

                def turn_hidden(n):
                    act.wait_ge(s["hT_ps"], n + 1)
                    if n >= 2:
                        act.wait_ge(s["y_ps"], n - 1)
                    act.activation(HT[:, n % 2].rearrange("p e i -> p (e i)"), PB[1][:], ACT.Copy) \
                        .then_inc(s["hT_sb"], 1)

                act.wait_ge(s["sc_v"], 1)
                for t in range(NT):
                    silu(EG * t)
                    act.wait_ge(s["o_v"], t + 1)
                    act.activation(SQ[:, t], O[:, t], ACT.Square).then_inc(s["sq_a"], 1)
                    turn_hidden(EG * t)
                    silu(EG * t + 1)
                    turn_hidden(EG * t + 1)
                    act.wait_ge(s["ogT_ps"], t + 1)
                    act.activation(OGT[:, :, t * P:(t + 1) * P], PB[0][:, 0:D].rearrange("p (k i) -> p k i", k=ND),
                                   ACT.Copy).then_inc(s["ogT_sb"], 1)

            @block.vector
            def _(dve):
                own = Own(dve, s["own_v"])

                def layernorm_stats(t0, t1):
                    for t in range(t0, t1):
                        own(dve.bn_stats(st[:, t], X[:, t]))
                    own.need(own.n)
                    for t in range(t0, t1):
                        own(dve.bn_aggr(mv[:, t], st[:, t]))
                    own.need(own.n)
                    dve.tensor_scalar(ve[:, t0:t1], mv[:, t0:t1, 1], LN_EPS, None, ALU.add).then_inc(s["var"], 1)

                def normalise(t):
                    return dve.tensor_scalar(XN[:, t], X[:, t], mv[:, t, 0:1], rstd[:, t:t + 1],
                                             ALU.subtract, ALU.mult)

                dve.wait_ge(s["x_in"], 16)
                layernorm_stats(0, NT)
                dve.wait_ge(s["pow_g"], 1)
                for t in range(NT):
                    normalise(t).then_inc(s["xn_tm"], 1)
                dve.wait_ge(s["xT_ps"], 1)
                dve.tensor_copy(XT[:, 1], PB[1][:]).then_inc(s["xT_sb"], 1)
                dve.wait_ge(s["sm_ps"], 1)
                dve.tensor_copy(SM[:].rearrange("p t h -> p (t h)"), PB[6][:, 0:NT * (H + E)]).then_inc(s["sm_tm"], 1)

                dve.wait_ge(s["sm_tm"], 1)
                dve.wait_ge(s["glog_a"], 1)
                own.now(dve.tensor_scalar(la[:], SM[:, :, 0:H], 0.0, None, ALU.min))
                own.now(dve.tensor_tensor(le[:], la[:], ll[:], ALU.subtract))
                dve.tensor_scalar(gt[:], le[:], 1.0 / 16.0, None, ALU.mult).then_inc(s["gt_v"], 1)
                own.now(dve.tensor_reduce(gm[:], SM[:, :, H:H + E], X_AXIS, ALU.max))
                dve.tensor_tensor(gc[:], SM[:, :, H:H + E], bc(gm[:], E), ALU.subtract).then_inc(s["gmax_v"], 1)

                def expert_weights():
                    dve.wait_ge(s["gexp_a"], 1)
                    own(dve.tensor_reduce(gs[:], ge[:], X_AXIS, ALU.add))
                    for t in range(NT):
                        own(dve.tensor_tensor(cmp1[:, t * E:(t + 1) * E], mid(ge[:, t], E), bc(ge[:, t], E), ALU.is_gt))
                        own(dve.tensor_tensor(cmp2[:, t * E:(t + 1) * E], mid(ge[:, t], E), bc(ge[:, t], E),
                                              ALU.is_equal))
                    own.need(own.n)
                    for t in range(NT):
                        own(dve.tensor_tensor(cmp2[:, t * E:(t + 1) * E], cmp2[:, t * E:(t + 1) * E], before[:],
                                              ALU.mult))
                    own.now(dve.reciprocal(gm[:], gs[:]))
                    own.now(dve.tensor_tensor(cmp1[:], cmp1[:], cmp2[:], ALU.add))
                    own.now(dve.tensor_reduce(gc[:].rearrange("p t e -> p (t e)"), cmp1[:], X_AXIS, ALU.add))
                    own.now(dve.tensor_scalar(gc[:], gc[:], 1.5, None, ALU.is_lt))
                    own.now(dve.tensor_tensor(gc[:], gc[:], ge[:], ALU.mult))
                    dve.tensor_tensor(SC[:], gc[:], bc(gm[:], E), ALU.mult).then_inc(s["sc_v"], 1)

                def turn(t):
                    dve.wait_ge(s["kT_ps"], t + 1)
                    dve.tensor_copy(KT[:, t].rearrange("p g i -> p (g i)"), PB[1][:]).then_inc(s["kT_sb"], 1)

                for t in range(NT):
                    dve.wait_ge(s["vg_ps"], t + 1)
                    dve.tensor_copy(VG[:, t], PB[4 + t % 2][:]).then_inc(s["vg_tm"], 1)
                    if t:
                        turn(t - 1)
                    if t == 1:
                        expert_weights()

                dve.wait_ge(s["ssq_a"], NT)
                dve.wait_ge(s["qk_tm"], NT)
                dve.tensor_scalar(ssq[:], ssq[:], 1.0 / D, RMS_EPS, ALU.mult, ALU.add).then_inc(s["ssq_v"], 1)
                turn(NT - 1)
                dve.wait_ge(s["pow_g"], 2)
                own(dve.tensor_tensor(fkv[:], rfac[:, :, 1], rfac[:, :, 2], ALU.mult))
                own.now(dve.tensor_scalar(fq[:], rfac[:, :, 0], HD ** -0.5, None, ALU.mult))
                dve.wait_ge(s["er_a"], 1)
                for t in range(NT):
                    dve.tensor_scalar(v1[:, t], VG[:, t, 0:D], fkv[:, t:t + 1], None, ALU.mult).then_inc(s["v1_v"], 1)
                for t in range(NT):
                    dve.wait_ge(s["v1_v"], t + 1)
                    dve.tensor_tensor(v2[:, t].rearrange("p (h e) -> p h e", h=H),
                                      v1[:, t].rearrange("p (h e) -> p h e", h=H), bc(ER[:, 0, t], HD), ALU.mult) \
                        .then_inc(s["v2_v"], 1)

                def state(t):
                    dve.wait_ge(s["kv_ps"], t + 1)
                    chunks = range(2 if t < NT - 1 else 1)
                    for c in chunks:
                        q = dve.tensor_tensor(kvm[:, c].rearrange("p (g c) -> p g c", g=HG),
                                              PB[(3, 1)[c]][:, 0:D].rearrange("p (g c) -> p g c", g=HG),
                                              mid(bdmask[:], HG), ALU.mult)
                    q.then_inc(s["kvm_v"], 1)
                    dve.wait_ge(s["kvm_v"], t + 1)
                    for c in chunks:
                        n = 2 * t + c
                        if n:
                            dve.wait_ge(s["S_v"], n)
                        own.now(dve.tensor_tensor(sdec[:].rearrange("p (h e) -> p h e", h=H),
                                                  S[:, n].rearrange("p (h e) -> p h e", h=H),
                                                  bc(ER[:, 2 + c, t], HD), ALU.mult))
                        dve.tensor_tensor(S[:, n + 1], sdec[:], kvm[:, c], ALU.add).then_inc(s["S_v"], 1)

                def decayed(t):
                    dve.wait_ge(s["sc_ps"], t + 1)
                    dve.wait_ge(s["dec_g"], t + 1)
                    if t >= 2:
                        dve.wait_ge(s["o_ps"], t - 1)
                    for r in range(4):
                        q = dve.tensor_tensor(AT[:, t % 2, r], PB[4 + r][:, 0:HG * CH].rearrange("p (g i) -> p g i", g=HG),
                                              dec[:, t].rearrange("p (g r) i -> p r g i", r=4)[:, r], ALU.mult)
                    q.then_inc(s["at_v"], 1)

                def hidden(n):
                    t, g = divmod(n, EG)
                    dve.wait_ge(s["hs_a"], n + 1)
                    if n >= 2:
                        dve.wait_ge(s["hT_ps"], n - 1)
                    for e in range(4):
                        q = dve.scalar_tensor_tensor(out=HH[:, n % 2, e], in0=PB[3][:, e * HID:(e + 1) * HID],
                                                     scalar=SC[:, t, 4 * g + e:4 * g + e + 1], in1=HS[:, n % 2, e],
                                                     op0=ALU.mult, op1=ALU.mult)
                    q.then_inc(s["h_v"], 1)

                def add_experts(n):
                    t = n // EG
                    if n % EG:
                        dve.wait_ge(s["y_v"], n)
                    dve.wait_ge(s["y_ps"], n + 1)
                    dve.tensor_tensor(X[:, t], X[:, t], PB[1][:, 0:D], ALU.add).then_inc(s["y_v"], 1)

                def next_input(t):
                    dve.wait_ge(s["pow_g"], 4 + 2 * t)
                    normalise(t).then_inc(s["xn2_v"], 1)
                    dve.wait_ge(s["xn2_v"], t + 1)
                    dve.tensor_tensor_reduce(prod[:, t], XN[:, t], tok[:], 1.0, 0.0, ALU.mult, ALU.add,
                                             S2[:, t:t + 1]).then_inc(s["s_v"], 1)

                dve.wait_ge(s["sc_v"], 1)
                decayed(0)
                state(0)
                for t in range(NT):
                    hidden(EG * t)
                    if t:
                        next_input(t - 1)
                    dve.wait_ge(s["o_ps"], t + 1)
                    o = O[:, t].rearrange("p (h e) -> p h e", h=H)
                    own.now(dve.tensor_tensor(o, PB[0][:, D:2 * D].rearrange("p (h e) -> p h e", h=H),
                                              bc(ER[:, 1, t], HD), ALU.mult))
                    own.now(dve.tensor_tensor(O[:, t], O[:, t], PB[0][:, 0:D], ALU.add))
                    dve.tensor_scalar(O[:, t], O[:, t], fq[:, t:t + 1], None, ALU.mult).then_inc(s["o_v"], 1)
                    dve.wait_ge(s["sq_a"], t + 1)
                    own.now(dve.tensor_reduce(hs[:, t], SQ[:, t].rearrange("p (h e) -> p h e", h=H), X_AXIS, ALU.add))
                    dve.tensor_scalar(hs[:, t], hs[:, t], 1.0 / HD, RMS_EPS, ALU.mult, ALU.add).then_inc(s["hs_v"], 1)
                    hidden(EG * t + 1)
                    dve.wait_ge(s["pow_g"], 3 + 2 * t)
                    own.now(dve.tensor_tensor(o, o, bc(hr[:, t], HD), ALU.mult))
                    if t == 0:
                        dve.wait_ge(s["sg_a"], 1)
                    dve.tensor_tensor(O[:, t], O[:, t], SG[:, t], ALU.mult).then_inc(s["og_v"], 1)
                    add_experts(EG * t)
                    if t < NT - 1:
                        decayed(t + 1)
                    add_experts(EG * t + 1)
                    dve.wait_ge(s["y_v"], EG * t + 2)
                    dve.wait_ge(s["wo_ps"], t + 1)
                    dve.tensor_tensor(X[:, t], X[:, t], PB[0][:, D:2 * D], ALU.add).then_inc(s["x1_v"], 1)
                    if t < NT - 1:
                        state(t + 1)
                    dve.wait_ge(s["x1_v"], t + 1)
                    layernorm_stats(t, t + 1)
                next_input(NT - 1)
          clear(nc, s)


def routing(nc, scr, PB, const):
    with ExitStack() as ctx:
        def sb(name, shape):
            return ctx.enter_context(nc.sbuf_tensor(name, [P, *shape], F32))

        s0, es, mins, part = sb("s0", [B, NT]), sb("es", [B, NT]), sb("mins", [B, NT]), sb("part", [B])
        first, kinv, keys = sb("first", [B]), sb("kinv", [P]), sb("keys", [B, NT])
        rows = sb("rows", [P])
        s = {n: ctx.enter_context(nc.semaphore("r_" + n)) for n in
             "s_in const_g es_a mins_v part_v r_ps keys_v rows_ps rows_v stored".split()}
        with nc.Block() as block:
            @block.sync
            def _(sp):
                sp.dma_start(s0[:], scr["s"][:].rearrange("b p t -> p b t")).then_inc(s["s_in"], 16)
                sp.wait_ge(s["keys_v"], 1)
                sp.dma_start(scr["key"][:].rearrange("b p t -> p b t"), keys[:]).then_inc(s["stored"], 16)
                sp.wait_ge(s["rows_v"], 1)
                sp.dma_start(scr["keyrow"][:].rearrange("b (t p) -> (b t) p", p=P), rows[0:B * NT]) \
                  .then_inc(s["stored"], 16)
                sp.wait_ge(s["stored"], 32)

            @block.gpsimd
            def _(pool):
                pool.memset(first[:], T / K_FETCH).then_inc(s["const_g"], 1)
                pool.memset(kinv[:], 1.0 / K_FETCH).then_inc(s["const_g"], 1)

            @block.scalar
            def _(act):
                act.wait_ge(s["s_in"], 16)
                act.activation(es[:], s0[:], ACT.Exp).then_inc(s["es_a"], 1)

            @block.tensor
            def _(pe):
                pe.wait_ge(s["const_g"], 2)
                for i in range(1, ROUTE_ITERS):
                    pe.wait_ge(s["part_v"], i)
                    pe.matmul(PB[i % 2][:, 0:B], kinv[:], part[:], start=True, stop=True).then_inc(s["r_ps"], 1)
                pe.wait_ge(s["keys_v"], 1)
                pe.transpose(PB[2][0:B * NT, 0:P], keys[:].rearrange("p b t -> p (b t)"), const["ident"][:]) \
                  .then_inc(s["rows_ps"], 1)

            @block.vector
            def _(dve):
                dve.wait_ge(s["es_a"], 1)
                dve.wait_ge(s["const_g"], 2)
                for i in range(1, ROUTE_ITERS + 1):
                    if i > 1:
                        dve.wait_ge(s["r_ps"], i - 1)
                    r = first[:] if i == 1 else PB[(i - 1) % 2][:, 0:B]
                    if i == ROUTE_ITERS:
                        dve.tensor_tensor(keys[:], es[:], bc(r, NT), ALU.min).then_inc(s["keys_v"], 1)
                        break
                    dve.tensor_tensor(mins[:], es[:], bc(r, NT), ALU.min).then_inc(s["mins_v"], 1)
                    dve.wait_ge(s["mins_v"], i)
                    dve.tensor_reduce(part[:], mins[:], X_AXIS, ALU.add).then_inc(s["part_v"], 1)
                dve.wait_ge(s["rows_ps"], 1)
                dve.tensor_copy(rows[0:B * NT], PB[2][0:B * NT, 0:P]).then_inc(s["rows_v"], 1)
        clear(nc, s)


def merged(*streams):
    at = sorted((i / len(s), n, i) for n, s in enumerate(streams) for i in range(len(s)))
    return [streams[n][i] for _, n, i in at]


def layer1(nc, out, w, scr, PB, const, load_ln_exp):
    SLOTS = 3
    NSC = DS * 2
    TILES = 2 * NT
    ITEMS = 2 * NT + NT * AH

    def tile_of(m):
        return m // 2 if m < 2 * NT else NT + (m - 2 * NT) // AH

    def last_of_tile(m):
        return 0 <= m < ITEMS and (m == ITEMS - 1 or tile_of(m + 1) != tile_of(m))

    STEPS = ITEMS + 7
    ADD_DVE = 2

    def out_bank(t):
        return 3 + (ITEMS - 3 + t // 2) % 3

    def added_by_dve(n):
        return n // 2 % ADD_DVE == 0

    def adds(n, dve):
        return sum(added_by_dve(i) == dve for i in range(n))

    projections = [(kind, what, i) for kind in range(2) for what in "qkv" for i in range(4)]
    proj = [("proj", i) for i in range(len(projections))]
    LATE = 9
    others = proj + [("att", q) for q in range(STEPS)]
    plan = merged([("scan", n) for n in range(NSC + 2)], others[:-LATE]) + others[-LATE:]

    with ExitStack() as ctx:
        def sb(name, shape):
            return ctx.enter_context(nc.sbuf_tensor(name, [P, *shape], F32))

        Win, Wx, Wout = sb("Win", [ND, 2 * DI]), sb("Wx", [NB, 2 * DS + 1]), sb("Wout", [NB, D])
        cw, cb, Wdt, bdt, Dp = sb("cw", [NB, CONV]), sb("cb", [NB]), sb("Wdt", [NB]), sb("bdt", [NB]), sb("Dp", [NB])
        A = sb("A", [NB, DS])
        Wq, Wk, Wv = ([sb(f"W{n}{i}", [ND, HIDA]) for i in range(2)] for n in "qkv")
        Wo = [sb(f"Wao{i}", [NA, D]) for i in range(2)]
        gamma = sb("gamma", [2, ND])
        before = sb("before1", [T + 3 * P])
        half = sb("half1", [NT])
        X, XN = sb("X1", [NT, D]), sb("XN1", [NT, D])
        XT, XRT = sb("XT1", [ND, T]), sb("XRT", [ND, T])
        XR = sb("XR", [NT, D])
        O, OT = XR[:, 0:2].rearrange("p t d -> p (t d)"), XR[:, 2:4].rearrange("p t d -> p (t d)")
        U, SZ, DEL, DU = (sb(n, [NB, T]) for n in ("U", "SZ", "DEL", "DU"))
        YA = U
        pool_of_probs = sb("probs", [NB * (T + CONV - 1)])
        XP = pool_of_probs[:].rearrange("p (b t) -> p b t", b=NB)
        PR = pool_of_probs[:, 0:2 * T].rearrange("p (a t) -> p a t", a=2)
        PT = pool_of_probs[:, 2 * T:4 * T].rearrange("p (a t) -> p a t", a=2)
        SSM = sb("SSM", [T])
        BC = sb("BC", [SLOTS, 2, T])
        Wxdt = sb("Wxdt", [NB, P])
        DA, HB2, HC2 = sb("DA", [2, 2, T]), sb("HB", [2, 2, T]), sb("HC", [2, 2, T])
        HB = [HB2[:, 0], HB2[:, 1], XT[:]]
        HC = [HC2[:, 0], HC2[:, 1], XN[:].rearrange("p (j t) d -> p j (t d)", j=2)]
        KR, KC = sb("KR", [T]), sb("KC", [NT])
        ahead, ties, sel = sb("ahead", [NT]), sb("ties", [NT]), sb("sel", [NT])
        ssq, fx = sb("ssq1", [NT]), sb("fx", [NT])
        Q, K, V = ([sb(f"{n}{i}", [4, T]) for i in range(2)] for n in ("Qa", "Ka", "Va"))
        act_junk, KJ = sb("act_junk", [2, D]), HC2[:, 0]
        nmax, sums, rec = sb("nmax", [3, 4]), sb("sums", [TILES, AH]), sb("rec", [TILES, AH])

        names = """w_in own_v own_a own_g x_in xn_in key_in xT_ps xT_sb ssq_a ssq_v pow_g xr_v xrT_ps xrT_sb
            in_ps in_a conv_v u_a ssm_ps ssm_a ssm_st dt_ps z_v abs_a pad_g soft_a del_v du_v wout_v
            bc_in0 bc_in1 bc_in2 dA_a dbu_g scan_v hc_v skip_v add_v add_g
            pj_ps pj_a pj_v s_ps max_v exp_a pt_ps pt_a av_ps on_v ot_ps ot_a yo_ps yo_v ym_v y_ps x_v stored"""
        s = {n: ctx.enter_context(nc.semaphore("b_" + n)) for n in names.split()}

        loaded = []
        with nc.Block() as block:
            @block.sync
            def _(sp):
                rows = "(k p) n -> p k n"
                loads = [
                    (Win[:], w["L1_attn_W_in"].rearrange(rows, p=P)),
                    (Wx[:], w["L1_attn_W_x"].rearrange(rows, p=P)),
                    (Wout[:], w["L1_attn_W_out"].rearrange(rows, p=P)),
                    (cw[:], w["L1_attn_conv_w"].rearrange("(k p) o n -> p k (o n)", p=P)),
                    (cb[:], w["L1_attn_conv_b"]),
                    (Wdt[:], w["L1_attn_W_dt"]),
                    (bdt[:], w["L1_attn_b_dt"]),
                    (Dp[:], w["L1_attn_D_param"]),
                    (A[:], w["L1_attn_A_log"].rearrange(rows, p=P)),
                    (Wq[0][:], w["L1_ffn_wq_light"].rearrange(rows, p=P)),
                    (Wk[0][:], w["L1_ffn_wkv_light"][:, 0:HIDA].rearrange(rows, p=P)),
                    (Wv[0][:], w["L1_ffn_wkv_light"][:, HIDA:].rearrange(rows, p=P)),
                    (Wo[0][:], w["L1_ffn_wo_light"].rearrange(rows, p=P)),
                    (Wq[1][:], w["L1_ffn_wq_heavy"].rearrange(rows, p=P)),
                    (Wo[1][:], w["L1_ffn_wo_heavy"].rearrange(rows, p=P)),
                    (gamma[:, 0], w["L1_ffn_gamma_light"]),
                    (gamma[:, 1], w["L1_ffn_gamma_heavy"]),
                ]
                for k in range(ND):
                    kv = w["L1_ffn_wkv_heavy"][k * P:(k + 1) * P].rearrange("p (h c d) -> p h c d", c=2, d=DH)
                    for c, dst in enumerate((Wk[1], Wv[1])):
                        loads.append((dst[:, k].rearrange("p (h d) -> p h d", d=DH), kv[:, :, c]))
                for dst, src in loads:
                    sp.dma_start(dst, src).then_inc(s["w_in"], 16)
                sp.wait_ge(s["w_in"], 16 * len(loads))
                loaded.append(16 * len(loads))

            @block.gpsimd
            def _(pool):
                own = Own(pool, s["own_g"])
                own(pool.memset(half[:], -0.5))
                own(pool.memset(DA[:], 0.0))
                own.now(pool.memset(before[:], 1.0))
                own.now(pool.affine_select(out=before[:], in_=before[:], compare_op=ALU.is_gt, fill=0.0,
                                           base=3 * P, pattern=[[-1, T + 3 * P]], channel_multiplier=1))

            @block.scalar
            def _(act):
                act.wait_ge(s["w_in"], loaded[0])
                act.activation(A[:], A[:], ACT.Exp).then_inc(s["own_a"], 1)

            @block.vector
            def _(dve):
                own = Own(dve, s["own_v"])
                dve.wait_ge(s["own_a"], 1)
                own(dve.tensor_scalar(A[:], A[:], -1.0, None, ALU.mult))
                for k in range(NB):
                    own(dve.tensor_copy(Wxdt[:, k], Wx[:, k, 0:1].broadcast_to([P, P])))
                for i in range(2):
                    for W in (Wq[i], Wk[i], Wv[i]):
                        for k in range(ND):
                            own(dve.tensor_scalar(W[:, k], W[:, k], gamma[:, i, k:k + 1], None, ALU.mult))
                own.need(own.n)
        clear(nc, s)

        ident = const["ident"]
        with nc.Fori(0, B) as b:
          with nc.Block() as block:
            @block.sync
            def _(sp):
                for dst, name, sem in ((XN, "xn2", "xn_in"), (X, "x1", "x_in")):
                    sp.dma_start(dst[:], scr[name][bass.ds(b, 1), :, :].rearrange("o (t p) d -> p (o t) d", p=P)) \
                      .then_inc(s[sem], 16)
                sp.dma_start(KC[:], scr["key"][bass.ds(b, 1), :, :].rearrange("o p t -> p (o t)")) \
                  .then_inc(s["key_in"], 16)
                sp.dma_start(KR[:], scr["keyrow"][bass.ds(b, 1), :].broadcast_to([P, T])).then_inc(s["key_in"], 16)
                sp.wait_ge(s["ssm_a"], 1)
                sp.dma_start(scr["ssm"][:], SSM[0:2 * DS + 1]).then_inc(s["ssm_st"], 16)
                sp.wait_ge(s["ssm_st"], 16)
                for st in range(DS):
                    if st >= SLOTS:
                        sp.wait_ge(s["dbu_g"], 2 * (st - SLOTS + 1))
                        sp.wait_ge(s["hc_v"], 2 * (st - SLOTS + 1))
                    sp.dma_start(BC[:, st % SLOTS], scr["ssm"][1 + st:2 * DS + 1:DS, :].unsqueeze(0)
                                 .broadcast_to([P, 2, T])).then_inc(s[f"bc_in{st % SLOTS}"], 16)
                for t in range(NT):
                    if t < NT - 1:
                        sp.wait_ge(s["wout_v"], t + 1)
                    else:
                        sp.wait_ge(s["x_v"], 1)
                    sp.dma_start(out[bass.ds(b, 1), t * P:(t + 1) * P, :].rearrange("o p d -> p (o d)"), X[:, t]) \
                      .then_inc(s["stored"], 16)
                sp.wait_ge(s["stored"], 16 * NT)

            def bc_loaded(eng, st):
                eng.wait_ge(s[f"bc_in{st % SLOTS}"], 16 * (st // SLOTS + 1))

            def add_state(eng, n, done):
                st, g = divmod(n, 2)
                eng.wait_ge(s["hc_v"], n + 1)
                if st:
                    dve = added_by_dve(n - 2)
                    eng.wait_ge(s["add_v" if dve else "add_g"], adds(n - 1, dve))
                eng.tensor_tensor(YA[:, 2 * g:2 * g + 2], YA[:, 2 * g:2 * g + 2], HC[n % 3], ALU.add) \
                   .then_inc(s[done], 1)

            @block.gpsimd
            def _(pool):
                pool.memset(XP[:, :, 0:CONV - 1], 0.0).then_inc(s["pad_g"], 1)
                pool.wait_ge(s["ssq_v"], 1)
                pool.tensor_tensor(fx[:], ssq[:], half[:], ALU.pow).then_inc(s["pow_g"], 1)
                for n in range(NSC + 2):
                    if n < NSC:
                        st, g = divmod(n, 2)
                        bc_loaded(pool, st)
                        if n < 2:
                            pool.wait_ge(s["du_v"], 2 * n + 2)
                        if n >= 3:
                            pool.wait_ge(s["hc_v"], n - 2)
                        pool.tensor_tensor(HB[n % 3], DU[:, 2 * g:2 * g + 2], mid(BC[:, st % SLOTS, 0], 2),
                                           ALU.mult).then_inc(s["dbu_g"], 1)
                    if n == 2:
                        pool.wait_ge(s["skip_v"], NB)
                    if n >= 2 and not added_by_dve(n - 2):
                        add_state(pool, n - 2, "add_g")

            @block.tensor
            def _(pe):
                def mm(out, lhsT, rhs, start=True, stop=True):
                    return pe.matmul(out, lhsT, rhs, start=start, stop=stop)

                pe.wait_ge(s["xn_in"], 16)
                for t in range(NT):
                    for k in range(ND):
                        q = pe.transpose(PB[k][:, t * P:(t + 1) * P], XN[:, t, k * P:(k + 1) * P], ident[:])
                q.then_inc(s["xT_ps"], 1)
                pe.wait_ge(s["xT_sb"], 2)
                for n in range(2 * NB):
                    if n == NB:
                        for t in range(NT):
                            pe.wait_ge(s["xr_v"], t + 1)
                            for k in range(ND):
                                q = pe.transpose(PB[2 + k][:, t * P:(t + 1) * P], XR[:, t, k * P:(k + 1) * P],
                                                 ident[:])
                        q.then_inc(s["xrT_ps"], 1)
                    if n >= NB:
                        pe.wait_ge(s["in_a"], n - 3)
                    for k in range(ND):
                        q = mm(PB[4 + n % 4][:], Win[:, k, n * P:(n + 1) * P], XT[:, k], k == 0, k == ND - 1)
                    q.then_inc(s["in_ps"], 1)
                for k in range(NB):
                    pe.wait_ge(s["u_a"], k + 1)
                    q = mm(PB[1][0:2 * DS + 1], Wx[:, k], U[:, k], k == 0, k == NB - 1)
                q.then_inc(s["ssm_ps"], 1)
                for k in range(NB):
                    q = mm(PB[0][:], Wxdt[:, k], U[:, k], k == 0, k == NB - 1)
                q.then_inc(s["dt_ps"], 1)
                pe.wait_ge(s["xrT_sb"], 2)

                def project(i):
                    kind, what, j = projections[i]
                    if i < 4:
                        pe.wait_ge(s["in_a"], 2 * NB)
                    else:
                        pe.wait_ge(s["pj_v" if i % 2 else "pj_a"], (i - 4) // 2 + 1)
                    for k in range(ND):
                        if what == "v":
                            q = mm(PB[2 + i % 4][:], XRT[:, k, j * P:(j + 1) * P], Wv[kind][:, k], k == 0, k == ND - 1)
                        else:
                            W = (Wq if what == "q" else Wk)[kind]
                            q = mm(PB[2 + i % 4][:], W[:, k, j * P:(j + 1) * P], XRT[:, k], k == 0, k == ND - 1)
                    q.then_inc(s["pj_ps"], 1)

                def attend(q):
                    m = q
                    if m < ITEMS:
                        par, bank = m % 2, PB[3 + m % 3]
                        rows = slice(DH * par, DH * (par + 1))
                        if m == 0:
                            pe.wait_ge(s["pj_a"], len(proj) // 2)
                            pe.wait_ge(s["pj_v"], len(proj) // 2)
                        if m >= 3:
                            pe.wait_ge(s["exp_a"], m - 2)
                        if m < 2 * NT:
                            cols = slice(m // 2 * P, (m // 2 + 1) * P)
                            for j in range(4):
                                i = mm(bank[:, j * P:(j + 1) * P], Q[0][rows, j, cols], K[0][rows, j, cols])
                        else:
                            t, h = divmod(m - 2 * NT, AH)
                            i = mm(bank[:], Q[1][rows, h // 2, t * P:(t + 1) * P], K[1][rows, h // 2])
                        i.then_inc(s["s_ps"], 1)
                    m = q - 2
                    if 0 <= m < ITEMS:
                        pe.wait_ge(s["exp_a"], m + 1)
                        if m >= 2:
                            pe.wait_ge(s["pt_a"], m - 1)
                        for j in range(4):
                            i = pe.transpose(PB[6 + m % 2][:, j * P:(j + 1) * P], PR[:, m % 2, j * P:(j + 1) * P],
                                             ident[:])
                        i.then_inc(s["pt_ps"], 1)
                    m = q - 3
                    if 0 <= m < ITEMS:
                        a = tile_of(m)
                        pe.wait_ge(s["pt_a"], m + 1)
                        if a >= 2 and a != tile_of(m - 1):
                            pe.wait_ge(s["on_v"], a - 1)
                        for j in range(4):
                            if m < 2 * NT:
                                h = m % 2 + 2 * j
                                i = mm(PB[1 + a % 2][:, h * DH:(h + 1) * DH], PT[:, m % 2, j * P:(j + 1) * P],
                                       V[0][:, m // 2, h * DH:(h + 1) * DH])
                            else:
                                h = (m - 2 * NT) % AH
                                i = mm(PB[1 + a % 2][:, h * DH:(h + 1) * DH], PT[:, m % 2, j * P:(j + 1) * P],
                                       V[1][:, j, h * DH:(h + 1) * DH], j == 0, j == 3)
                        i.then_inc(s["av_ps"], 1)
                    if last_of_tile(q - 5):
                        a = tile_of(q - 5)
                        pe.wait_ge(s["on_v"], a + 1)
                        if a:
                            pe.wait_ge(s["yo_v"], a)
                        for j in range(NA):
                            i = pe.transpose(PB[0][:, j * P:(j + 1) * P], O[:, j * P:(j + 1) * P], ident[:])
                        i.then_inc(s["ot_ps"], 1)
                    if last_of_tile(q - 6):
                        a = tile_of(q - 6)
                        pe.wait_ge(s["ot_a"], a + 1)
                        for j in range(NA):
                            i = mm(PB[0][:, 0:D], OT[:, j * P:(j + 1) * P], Wo[a // NT][:, j], j == 0, j == NA - 1)
                        i.then_inc(s["yo_ps"], 1)

                def scan_out(t):
                    if t == 0:
                        pe.wait_ge(s["ym_v"], NB)
                    pe.wait_ge(s["exp_a"], ITEMS - 2 + t // 2)
                    for k in range(NB):
                        q = mm(PB[out_bank(t)][:, t % 2 * D:(t % 2 + 1) * D], DU[:, k, t * P:(t + 1) * P], Wout[:, k],
                               k == 0, k == NB - 1)
                    q.then_inc(s["y_ps"], 1)

                for what, i in plan:
                    if what == "proj":
                        project(i)
                    elif what == "att":
                        if i == 0:
                            pe.wait_ge(s["ssm_a"], 1)
                            pe.wait_ge(s["z_v"], NB)
                        attend(i)
                        if i in (ITEMS, ITEMS + 1):
                            scan_out(2 * (i - ITEMS))
                            scan_out(2 * (i - ITEMS) + 1)

            @block.scalar
            def _(act):
                own = Own(act, s["own_a"])

                def project(i):
                    if i % 2:
                        return
                    kind, what, j = projections[i]
                    act.wait_ge(s["pj_ps"], i + 1)
                    dst = {"q": Q, "k": K, "v": V}[what][kind]
                    act.activation(dst[:, j], PB[2 + i % 4][:], ACT.Copy, scale=DH ** -0.5 if what == "q" else 1.0) \
                        .then_inc(s["pj_a"], 1)

                act.wait_ge(s["xn_in"], 16)
                for t in range(NT):
                    if t >= 2:
                        act.wait_ge(s["ssq_a"], t - 1)
                    act.activation(act_junk[:, t % 2], XN[:, t], ACT.Square, accum_out=ssq[:, t:t + 1]) \
                        .then_inc(s["ssq_a"], 1)
                act.wait_ge(s["xT_ps"], 1)
                act.activation(XT[:, 0], PB[0][:], ACT.Copy).then_inc(s["xT_sb"], 1)
                for k in range(NB):
                    act.wait_ge(s["in_ps"], k + 1)
                    act.activation(XP[:, k, CONV - 1:], PB[4 + k][:], ACT.Copy)
                    act.activation(DEL[:, k], PB[4 + k][:], ACT.Identity, bias=cb[:, k:k + 1],
                                   scale=cw[:, k, CONV - 1:CONV]).then_inc(s["in_a"], 1)
                act.wait_ge(s["xrT_ps"], 1)
                for k in range(ND):
                    act.activation(XRT[:, k], PB[2 + k][:], ACT.Copy).then_inc(s["xrT_sb"], 1)
                for k in range(NB):
                    act.wait_ge(s["conv_v"], k + 1)
                    act.activation(U[:, k], DEL[:, k], ACT.Silu).then_inc(s["u_a"], 1)
                for k in range(NB):
                    act.wait_ge(s["in_ps"], NB + k + 1)
                    act.activation(SZ[:, k], PB[4 + k][:], ACT.Silu).then_inc(s["in_a"], 1)
                load_ln_exp(act)
                act.wait_ge(s["ssm_ps"], 1)
                act.activation(SSM[0:2 * DS + 1], PB[1][0:2 * DS + 1], ACT.Copy).then_inc(s["ssm_a"], 1)
                act.wait_ge(s["u_a"], NB)
                for g in range(NB // 2):
                    act.wait_ge(s["z_v"], 2 * g + 2)
                    e = DEL[:, 2 * g:2 * g + 2]
                    own.now(act.activation(e, DU[:, 2 * g:2 * g + 2], ACT.Abs))
                    own.now(act.activation(e, e, ACT.Exp, scale=-1.0))
                    act.activation(e, e, ACT.Ln, bias=1.0).then_inc(s["soft_a"], 1)

                def decay(n):
                    st, g = divmod(n, 2)
                    if n < 2:
                        act.wait_ge(s["del_v"], 2 * n + 2)
                    if n >= 2:
                        act.wait_ge(s["scan_v"], n - 1)
                    for j in range(2):
                        q = act.activation(DA[:, n % 2, j, 1:], DEL[:, 2 * g + j, 1:], ACT.Exp,
                                           scale=A[:, 2 * g + j, st:st + 1])
                    q.then_inc(s["dA_a"], 1)

                def attend(q):
                    m = q - 1
                    if 0 <= m < ITEMS:
                        act.wait_ge(s["max_v"], m + 1)
                        if m >= 2:
                            act.wait_ge(s["pt_ps"], m - 1)
                        par, bank, a = m % 2, PB[3 + m % 3], tile_of(m)
                        if m < 2 * NT:
                            for j in range(4):
                                i = act.activation(PR[:, par, j * P:(j + 1) * P], bank[:, j * P:(j + 1) * P],
                                                   ACT.Exp, bias=nmax[:, m % 3, j:j + 1],
                                                   accum_out=sums[:, a, par + 2 * j:par + 2 * j + 1])
                        else:
                            h = (m - 2 * NT) % AH
                            i = act.activation(PR[:, par], bank[:], ACT.Exp, bias=nmax[:, m % 3, 0:1],
                                               accum_out=sums[:, a, h:h + 1])
                        i.then_inc(s["exp_a"], 1)
                    m = q - 2
                    if 0 <= m < ITEMS:
                        act.wait_ge(s["pt_ps"], m + 1)
                        if m >= 2:
                            act.wait_ge(s["av_ps"], m - 1)
                        act.activation(PT[:, m % 2], PB[6 + m % 2][:], ACT.Copy).then_inc(s["pt_a"], 1)
                    if last_of_tile(q - 5):
                        act.wait_ge(s["ot_ps"], tile_of(q - 5) + 1)
                        act.activation(OT, PB[0][:], ACT.Copy).then_inc(s["ot_a"], 1)

                for what, i in plan:
                    if what == "proj":
                        project(i)
                    elif what == "att":
                        attend(i)
                    elif i < NSC:
                        decay(i)

            @block.vector
            def _(dve):
                own = Own(dve, s["own_v"])
                dve.wait_ge(s["xT_ps"], 1)
                dve.tensor_copy(XT[:, 1], PB[1][:]).then_inc(s["xT_sb"], 1)
                dve.wait_ge(s["ssq_a"], NT)
                dve.tensor_scalar(ssq[:], ssq[:], 1e-24, None, ALU.max).then_inc(s["ssq_v"], 1)
                dve.wait_ge(s["pow_g"], 1)
                dve.wait_ge(s["x_in"], 16)
                dve.wait_ge(s["xn_in"], 16)
                for t in range(NT):
                    dve.tensor_scalar(XR[:, t], XN[:, t], fx[:, t:t + 1], D ** 0.5, ALU.mult, ALU.mult) \
                        .then_inc(s["xr_v"], 1)
                dve.wait_ge(s["pad_g"], 1)
                for k in range(NB):
                    dve.wait_ge(s["in_a"], k + 1)
                    for c in range(CONV - 1):
                        i = dve.scalar_tensor_tensor(out=DEL[:, k], in0=XP[:, k, c:c + T], scalar=cw[:, k, c:c + 1],
                                                     in1=DEL[:, k], op0=ALU.mult, op1=ALU.add)
                        if c == CONV - 2:
                            i.then_inc(s["conv_v"], 1)
                        else:
                            own.now(i)

                dve.wait_ge(s["key_in"], 32)
                for t in range(NT):
                    own.need(own.n)
                    own(dve.tensor_scalar(KJ[:, 0], KR[:], KC[:, t:t + 1], None, ALU.is_gt, ALU.add,
                                          accum_out=ahead[:, t:t + 1]))
                    own(dve.scalar_tensor_tensor(out=KJ[:, 1], in0=KR[:], scalar=KC[:, t:t + 1],
                                                 in1=before[:, (3 - t) * P:(3 - t) * P + T],
                                                 op0=ALU.is_equal, op1=ALU.mult, accum_out=ties[:, t:t + 1]))
                own.need(own.n)
                own.now(dve.tensor_tensor(ahead[:], ahead[:], ties[:], ALU.add))
                own.now(dve.tensor_scalar(sel[:], ahead[:], NQ - 0.5, None, ALU.is_lt))

                dve.wait_ge(s["dt_ps"], 1)
                for k in range(NB):
                    dve.tensor_scalar(DU[:, k], PB[0][:], Wdt[:, k:k + 1], bdt[:, k:k + 1], ALU.mult, ALU.add) \
                        .then_inc(s["z_v"], 1)
                for g in range(NB // 2):
                    dve.wait_ge(s["soft_a"], g + 1)
                    pair = slice(2 * g, 2 * g + 2)
                    dve.scalar_tensor_tensor(out=DEL[:, pair], in0=DU[:, pair], scalar=0.0, in1=DEL[:, pair],
                                             op0=ALU.max, op1=ALU.add).then_inc(s["del_v"], 2)
                    dve.wait_ge(s["del_v"], 2 * g + 2)
                    dve.tensor_tensor(DU[:, pair], DEL[:, pair], U[:, pair], ALU.mult).then_inc(s["du_v"], 2)
                dve.wait_ge(s["du_v"], NB)
                for k in range(NB):
                    dve.tensor_scalar(YA[:, k], U[:, k], Dp[:, k:k + 1], None, ALU.mult).then_inc(s["skip_v"], 1)
                dve.wait_ge(s["skip_v"], NB)

                def project(i):
                    if i % 2 == 0:
                        return
                    kind, what, j = projections[i]
                    dve.wait_ge(s["pj_ps"], i + 1)
                    dst = {"q": Q, "k": K, "v": V}[what][kind]
                    if what == "q":
                        q = dve.tensor_scalar(dst[:, j], PB[2 + i % 4][:], DH ** -0.5, None, ALU.mult)
                    else:
                        q = dve.tensor_copy(dst[:, j], PB[2 + i % 4][:])
                    q.then_inc(s["pj_v"], 1)

                def gate():
                    dve.wait_ge(s["add_v"], adds(NSC, True))
                    dve.wait_ge(s["add_g"], adds(NSC, False))
                    for k in range(NB):
                        dve.tensor_tensor(DU[:, k], YA[:, k], SZ[:, k], ALU.mult).then_inc(s["ym_v"], 1)

                def scan_out():
                    dve.wait_ge(s["yo_v"], TILES - 1)
                    for t in range(NT):
                        dve.wait_ge(s["y_ps"], t // 2 * 2 + 2)
                        i = dve.tensor_tensor(X[:, t], X[:, t], PB[out_bank(t)][:, t % 2 * D:(t % 2 + 1) * D], ALU.add)
                        i.then_inc(s["wout_v"], 1)

                def scan(n):
                    dve.wait_ge(s["dA_a"], n + 1)
                    dve.wait_ge(s["dbu_g"], n + 1)
                    h = HB[n % 3].rearrange("p j t -> p (j t)")
                    dve.tensor_tensor_scan(h, DA[:, n % 2].rearrange("p j t -> p (j t)"), h, 0.0,
                                           ALU.mult, ALU.add).then_inc(s["scan_v"], 1)

                def times_c(n):
                    st = n // 2
                    dve.wait_ge(s["scan_v"], n + 1)
                    bc_loaded(dve, st)
                    if n >= 3 and added_by_dve(n - 3):
                        dve.wait_ge(s["add_v"], adds(n - 2, True))
                    elif n >= 3:
                        dve.wait_ge(s["add_g"], adds(n - 2, False))
                    dve.tensor_tensor(HC[n % 3], HB[n % 3], mid(BC[:, st % SLOTS, 1], 2), ALU.mult) \
                        .then_inc(s["hc_v"], 1)

                def attend(q):
                    m = q
                    if m < ITEMS:
                        dve.wait_ge(s["s_ps"], m + 1)
                        if m >= 3:
                            dve.wait_ge(s["exp_a"], m - 2)
                        if m < 2 * NT:
                            i = dve.tensor_reduce(nmax[:, m % 3], PB[3 + m % 3][:].rearrange("p (j i) -> p j i", j=4),
                                                  X_AXIS, ALU.max, negate=True)
                        else:
                            i = dve.tensor_reduce(nmax[:, m % 3, 0:1], PB[3 + m % 3][:], X_AXIS, ALU.max, negate=True)
                        i.then_inc(s["max_v"], 1)
                    m = q - 4
                    if last_of_tile(m):
                        a = tile_of(m)
                        dve.wait_ge(s["exp_a"], m + 1)
                        own.now(dve.reciprocal(rec[:, a], sums[:, a]))
                        if a >= NT:
                            own.now(dve.tensor_scalar(rec[:, a], rec[:, a], sel[:, a - NT:a - NT + 1], None, ALU.mult))
                        dve.wait_ge(s["av_ps"], m + 1)
                        if a:
                            dve.wait_ge(s["ot_ps"], a)
                        dve.tensor_tensor(O.rearrange("p (h d) -> p h d", h=AH),
                                          PB[1 + a % 2][:].rearrange("p (h d) -> p h d", h=AH), bc(rec[:, a], DH),
                                          ALU.mult).then_inc(s["on_v"], 1)
                    if last_of_tile(q - 6):
                        a = tile_of(q - 6)
                        dve.wait_ge(s["yo_ps"], a + 1)
                        if a == TILES - 1:
                            dve.wait_ge(s["wout_v"], NT)
                        elif a >= NT:
                            dve.wait_ge(s["yo_v"], a - NT + 1)
                        i = dve.tensor_tensor(X[:, a % NT], X[:, a % NT], PB[0][:, 0:D], ALU.add)
                        i.then_inc(s["x_v" if a == TILES - 1 else "yo_v"], 1)

                for what, i in plan:
                    if what == "proj":
                        project(i)
                    elif what == "att":
                        attend(i)
                        if i == ITEMS + 3:
                            scan_out()
                    else:
                        if i < NSC:
                            scan(i)
                        if 0 <= i - 1 < NSC:
                            times_c(i - 1)
                        if 0 <= i - 2 < NSC and added_by_dve(i - 2):
                            add_state(dve, i - 2, "add_v")
                        if i == NSC + 1:
                            gate()
          clear(nc, s)


def build(nc, out, w):
    x = w["L0_attn_x"]
    scr = {
        "x1": nc.dram_tensor("x1_scratch", [B, T, D], F32).ap(),
        "xn2": nc.dram_tensor("xn2_scratch", [B, T, D], F32).ap(),
        "s": nc.dram_tensor("s_scratch", [B, P, NT], F32).ap(),
        "key": nc.dram_tensor("key_scratch", [B, P, NT], F32).ap(),
        "keyrow": nc.dram_tensor("keyrow_scratch", [B, T], F32).ap(),
        "ssm": nc.dram_tensor("ssm_scratch", [2 * DS + 1, T], F32).ap(),
    }
    def load_ln_exp(act):
        act.add_instruction(mybir.InstLoadActFuncSet(name=nc.get_next_instruction_name(), act_func_set_id=LN_EXP_TABLE,
                                                     ins=[], outs=[]))

    with ExitStack() as ctx:
        PB = [ctx.enter_context(nc.psum_tensor(f"bank{i}", [P, 512], F32)) for i in range(8)]
        ident = ctx.enter_context(nc.sbuf_tensor("ident", [P, P], F32))
        made = ctx.enter_context(nc.semaphore("ident_made"))
        with nc.Block() as block:
            @block.gpsimd
            def _(pool):
                pool.memset(ident[:], 0.0).then_inc(made, 1)
                pool.wait_ge(made, 1)
                pool.affine_select(out=ident[:], in_=ident[:], compare_op=ALU.not_equal, fill=1.0, base=0,
                                   pattern=[[-1, P]], channel_multiplier=1).then_inc(made, 1)
                pool.wait_ge(made, 2)
        const = {"ident": ident}
        layer0(nc, x, w, scr, PB, const, load_ln_exp)
        routing(nc, scr, PB, const)
        layer1(nc, out, w, scr, PB, const, load_ln_exp)


_INS = ["L0_attn_x", "L0_attn_Wq", "L0_attn_Wk", "L0_attn_Wv", "L0_attn_Wg", "L0_attn_Wgt", "L0_attn_Wo",
        "L0_ffn_gate_w", "L0_ffn_w1", "L0_ffn_w2", "L0_ffn_w3", "L1_attn_W_in", "L1_attn_conv_w",
        "L1_attn_conv_b", "L1_attn_W_x", "L1_attn_W_dt", "L1_attn_b_dt", "L1_attn_A_log", "L1_attn_D_param",
        "L1_attn_W_out", "L1_ffn_gamma_light", "L1_ffn_wq_light", "L1_ffn_wkv_light", "L1_ffn_wo_light",
        "L1_ffn_q_routing_token", "L1_ffn_gamma_heavy", "L1_ffn_wq_heavy", "L1_ffn_wkv_heavy",
        "L1_ffn_wo_heavy"]
_TRANSPOSED = ("L1_attn_W_in", "L1_attn_W_x", "L1_attn_W_out", "L1_ffn_wkv_heavy")
_COLUMNS = ("L1_attn_conv_b", "L1_attn_W_dt", "L1_attn_b_dt", "L1_attn_D_param", "L1_ffn_gamma_light",
            "L1_ffn_gamma_heavy")


def kernel(**inputs):
    import concourse.bacc as bacc
    from concourse.bass_utils import run_bass_kernel_spmd

    nc = bacc.Bacc("TRN2", target_bir_lowering=False, num_devices=1)
    arrays, w = {}, {}
    for name in _INS:
        a = np.asarray(inputs[name])
        a = a.T if name in _TRANSPOSED else a.reshape(-1, P).T if name in _COLUMNS else a
        a = np.ascontiguousarray(a)
        arrays[f"in_{name}"] = a
        w[name] = nc.dram_tensor(f"in_{name}", a.shape, mybir.dt.from_np(a.dtype), kind="ExternalInput").ap()
    out = nc.dram_tensor("out", (B, T, D), F32, kind="ExternalOutput").ap()
    build(nc, out, w)
    r = run_bass_kernel_spmd(nc, [arrays], core_ids=[0])
    return r.results[0]["out"]
```
